# Optimizing a Trainium2 kernel written in Bass

```python
import numpy as np
import jax
import jax.numpy as jnp

def _softmax(x, axis=-1):
    return jax.nn.softmax(x, axis=axis)
def _gelu(x):
    return jax.nn.gelu(x, approximate=True)
def _silu(x):
    return jax.nn.silu(x)
def _sigmoid(x):
    return jax.nn.sigmoid(x)
def _layernorm(x, axis=-1, eps=1e-5):
    m = jnp.mean(x, axis=axis, keepdims=True)
    v = jnp.var(x, axis=axis, keepdims=True)
    return (x - m) / jnp.sqrt(v + eps)
def _scatter_add(tgt, idx, src, axis=0):
    return tgt.at[idx].add(src)
def _segment_sum(src, seg, n):
    return jax.ops.segment_sum(src, seg, n)

kernel_name = 'mk_conv_seq_d2_conv_nchw512_5f5937'

def setup_inputs(seed: int = 0):
    np.random.seed(seed)
    _w = jnp.asarray
    def _rec_inputs():
        import jax
        import jax.numpy as jnp
        _gk = jax.random.key(seed)
        x = -0.0001546 + 1 * jax.random.normal(jax.random.fold_in(_gk, 1), (2, 512, 256, 256), jnp.float32)
        return x
    x = _rec_inputs()
    def _L0_conv_setup():
        import jax, jax.numpy as jnp
        import numpy as np
        COORD_SIZE = 256
        HIDDEN = 512
        BATCH = 4

        def _coord_grid(h, w):
            y = jnp.linspace(-1.0, 1.0, h)
            x = jnp.linspace(-1.0, 1.0, w)
            yy, xx = jnp.meshgrid(y, x, indexing='ij')
            return jnp.stack([xx, yy], axis=0)
        key = jax.random.key(seed)
        k1, k2, k3 = jax.random.split(key, 3)
        x = jax.random.normal(k1, (BATCH, HIDDEN, COORD_SIZE, COORD_SIZE), dtype=jnp.float32)
        limit = np.sqrt(9.0 / 2.0)
        W = jax.random.uniform(k2, (HIDDEN, 2), minval=-limit, maxval=limit, dtype=jnp.float32)
        b = jax.random.normal(k3, (HIDDEN,), dtype=jnp.float32) * 0.01
        return {'x': x, 'W': W, 'b': b}
    _L0_conv_all = _L0_conv_setup()
    _L0_conv_in = {k: v for k, v in _L0_conv_all.items() if k in ('W', 'b', )}
    del _L0_conv_all

    def _L1_conv_setup():
        import jax, jax.numpy as jnp
        import numpy as np
        UP = 2
        DOWN = 2
        NEG_SLOPE = 0.2
        MARGIN = 10
        FLRELU_SCALE = np.float32(2.0 ** 0.5)
        UP_PAD = ((10 + 1) // 2 + UP - 1, 10 // 2)
        DOWN_PAD = ((10 + 1) // 2, 10 // 2)
        _FILT = np.array([0.0, 0.00398, -0.01884, -0.05155, 0.12443, 0.44197, 0.44197, 0.12443, -0.05155, -0.01884, 0.00398, 0.0], dtype=np.float32)
        _FILT = _FILT / _FILT.sum()

        def _fir1d(x, k, up, down, pad0, pad1, axis):
            N, C, H, W = x.shape
            xr = x.reshape(N * C, 1, H, W)
            K = k.shape[0]
            kf = k[::-1].astype(x.dtype)
            if axis == 3:
                w = kf.reshape(1, 1, 1, K)
                lhs_dil = (1, up)
                strides = (1, down)
                padding = ((0, 0), (pad0, pad1 + up - 1))
            else:
                w = kf.reshape(1, 1, K, 1)
                lhs_dil = (up, 1)
                strides = (down, 1)
                padding = ((pad0, pad1 + up - 1), (0, 0))
            y = jax.lax.conv_general_dilated(xr, w, window_strides=strides, padding=padding, lhs_dilation=lhs_dil, dimension_numbers=('NCHW', 'OIHW', 'NCHW'))
            return y.reshape(N, C, y.shape[2], y.shape[3])

        def _sep_upfirdn(x, k, up, down, pad):
            x = _fir1d(x, k, up, down, pad[0], pad[1], axis=3)
            x = _fir1d(x, k, up, down, pad[0], pad[1], axis=2)
            return x
        key = jax.random.key(seed)
        k_in = jax.random.fold_in(key, 0)
        return {'input': jax.random.normal(k_in, (8, 512, 64, 64), dtype=jnp.float32), 'bias': jnp.zeros((512,), dtype=jnp.float32), 'up_filter': jnp.asarray(_FILT), 'down_filter': jnp.asarray(_FILT)}
    _L1_conv_all = _L1_conv_setup()
    _L1_conv_in = {k: v for k, v in _L1_conv_all.items() if k in ('bias', 'up_filter', 'down_filter', )}
    del _L1_conv_all

    return {
        "x": x,
        "L0_conv_W": _L0_conv_in["W"],
        "L0_conv_b": _L0_conv_in["b"],
        "L1_conv_bias": _L1_conv_in["bias"],
        "L1_conv_up_filter": _L1_conv_in["up_filter"],
        "L1_conv_down_filter": _L1_conv_in["down_filter"],
    }

def reference(x, L0_conv_W, L0_conv_b, L1_conv_bias, L1_conv_up_filter, L1_conv_down_filter):
    import jax
    import jax.numpy as jnp
    def _L0_conv_ref(x, W, b):
        import jax, jax.numpy as jnp
        import numpy as np
        COORD_SIZE = 256
        HIDDEN = 512
        BATCH = 4

        def _coord_grid(h, w):
            y = jnp.linspace(-1.0, 1.0, h)
            x = jnp.linspace(-1.0, 1.0, w)
            yy, xx = jnp.meshgrid(y, x, indexing='ij')
            return jnp.stack([xx, yy], axis=0)
        coord = _coord_grid(x.shape[2], x.shape[3])
        lin = jnp.einsum('oc,chw->ohw', W, coord) + b[:, None, None]
        fourier = jnp.sin(lin)
        return x + fourier[None]

    def _L1_conv_ref(input, bias, up_filter, down_filter):
        import jax, jax.numpy as jnp
        import numpy as np
        UP = 2
        DOWN = 2
        NEG_SLOPE = 0.2
        MARGIN = 10
        FLRELU_SCALE = np.float32(2.0 ** 0.5)
        UP_PAD = ((10 + 1) // 2 + UP - 1, 10 // 2)
        DOWN_PAD = ((10 + 1) // 2, 10 // 2)
        _FILT = np.array([0.0, 0.00398, -0.01884, -0.05155, 0.12443, 0.44197, 0.44197, 0.12443, -0.05155, -0.01884, 0.00398, 0.0], dtype=np.float32)
        _FILT = _FILT / _FILT.sum()

        def _fir1d(x, k, up, down, pad0, pad1, axis):
            N, C, H, W = x.shape
            xr = x.reshape(N * C, 1, H, W)
            K = k.shape[0]
            kf = k[::-1].astype(x.dtype)
            if axis == 3:
                w = kf.reshape(1, 1, 1, K)
                lhs_dil = (1, up)
                strides = (1, down)
                padding = ((0, 0), (pad0, pad1 + up - 1))
            else:
                w = kf.reshape(1, 1, K, 1)
                lhs_dil = (up, 1)
                strides = (down, 1)
                padding = ((pad0, pad1 + up - 1), (0, 0))
            y = jax.lax.conv_general_dilated(xr, w, window_strides=strides, padding=padding, lhs_dilation=lhs_dil, dimension_numbers=('NCHW', 'OIHW', 'NCHW'))
            return y.reshape(N, C, y.shape[2], y.shape[3])

        def _sep_upfirdn(x, k, up, down, pad):
            x = _fir1d(x, k, up, down, pad[0], pad[1], axis=3)
            x = _fir1d(x, k, up, down, pad[0], pad[1], axis=2)
            return x
        out = input + bias[None, :, None, None]
        upf = up_filter * UP
        out = _sep_upfirdn(out, upf, UP, 1, UP_PAD)
        out = jax.nn.leaky_relu(out, NEG_SLOPE) * FLRELU_SCALE
        out = _sep_upfirdn(out, down_filter, 1, DOWN, DOWN_PAD)
        m = (MARGIN * UP - MARGIN * DOWN) // 2
        if m > 0:
            out = out[:, :, m:-m, m:-m]
        return out

    def _gn(v, G=32, eps=1e-5):
        B_, C_, H_, W_ = v.shape
        g = v.reshape(B_, G, C_ // G, H_, W_)
        m = jnp.mean(g, axis=(2, 3, 4), keepdims=True)
        s = jnp.var(g, axis=(2, 3, 4), keepdims=True)
        return ((g - m) / jnp.sqrt(s + eps)).reshape(v.shape)

    def _ln_c(v, eps=1e-6):
        m = jnp.mean(v, axis=1, keepdims=True)
        s = jnp.var(v, axis=1, keepdims=True)
        return (v - m) / jnp.sqrt(s + eps)

    def _ln_t(v, eps=1e-5):
        m = jnp.mean(v, axis=-1, keepdims=True)
        s = jnp.var(v, axis=-1, keepdims=True)
        return (v - m) / jnp.sqrt(s + eps)

    def _to_tokens(v):
        B_, C_, H_, W_ = v.shape
        return v.reshape(B_, C_, H_ * W_).transpose(0, 2, 1)
    def _from_tokens(t, like):
        B_, C_, H_, W_ = like.shape
        return t.transpose(0, 2, 1).reshape(B_, C_, H_, W_)

    x = _L0_conv_ref(x, L0_conv_W, L0_conv_b)
    x = _L1_conv_ref(x, L1_conv_bias, L1_conv_up_filter, L1_conv_down_filter)
    return x


_drawn_inputs = setup_inputs


def setup_inputs(seed=0):
    import zlib

    import numpy as np

    out = dict(_drawn_inputs(seed))
    spreads = {'L1_conv_bias': (0.0, 0.1)}
    factors = {'L0_conv_b': 8.0}
    for name, (base, spread) in spreads.items():
        noise = np.random.default_rng([zlib.crc32(name.encode()), seed]).standard_normal(out[name].shape)
        drawn = base * np.exp(spread * noise) if base else spread * noise
        out[name] = jnp.asarray(drawn.astype(out[name].dtype))
    for name, factor in factors.items():
        out[name] = (out[name] * factor).astype(out[name].dtype)
    return out
```

```python
import concourse.bass as bass
from concourse import mybir
from contextlib import ExitStack
import math


def filtered_lrelu_kernel(nc, x, W, b, bias, up_filter, down_filter, out):
    f32 = mybir.dt.float32
    f32r = mybir.dt.float32r
    ALU = mybir.AluOpType
    ACT = mybir.ActivationFunctionType

    BATCH, C, H, WID = x.shape
    TAPS = up_filter.shape[0]
    P = 128
    assert BATCH == 2 and H == 2 * P and WID == 2 * P and TAPS == 12
    HT = H // P
    UP = 2 * H
    UT = UP // P
    IMAGES = BATCH * C

    UPW = 268
    UP_SPAN = [(0, 262, 6), (250, 512, 0)]
    DNW = 72
    DN_SPAN = [(0, 68, 4), (60, 132, 0), (124, 196, 0), (188, 256, 0)]

    SLOPE = 0.2
    GAIN = math.sqrt(2.0)

    TWO_PI_A = 6.28125
    TWO_PI_B = 0.0019350051879882812
    TWO_PI_C = 2.0 * math.pi - TWO_PI_A - TWO_PI_B
    ROUND = 1.5 * 2.0 ** 23
    PI_DOWN = 3.1415925

    CP = min(P, C)
    CT = C // CP
    ROWS = 10

    trig_dram = nc.dram_tensor("trig_dram", [C, ROWS, H + WID], f32).ap()
    trig_store = trig_dram.rearrange("(p t) r n -> t p (r n)", t=CT)

    ctx = ExitStack()
    with ctx:
        def sb(name, shape, dt=f32):
            return ctx.enter_context(nc.sbuf_tensor(name, shape, dt))

        def pb(name, shape):
            return ctx.enter_context(nc.psum_tensor(name, shape, f32))

        def sem(name):
            return ctx.enter_context(nc.semaphore(name))

        up_taps = sb("up_taps", [P, TAPS])
        down_taps = sb("down_taps", [P, TAPS])
        w_cols = sb("w_cols", [CP, CT, 2])
        b_cols = sb("b_cols", [CP, CT])
        bias_cols = sb("bias_cols", [CP, CT])
        bias_high = sb("bias_high", [CP, CT], f32r)
        bias_low = sb("bias_low", [CP, CT])
        up_ones = sb("up_ones", [P, 280])
        down_ones = sb("down_ones", [P, 156])
        up_band = sb("up_band", [P, UPW])
        down_band = sb("down_band", [P, DNW])
        coord = sb("coord", [CP, H])
        ones = sb("ones", [CP, H])
        phase = sb("phase", [CP, 2, H])
        turns = sb("turns", [CP, 2, 2 * H])
        angle = sb("angle", [CP, 2, 2 * H])
        trig = sb("trig", [CP, 2, 2, H])
        trig_rows = sb("trig_rows", [CP, ROWS, H + WID], f32r)
        up_high = sb("up_high", [P, UPW], f32r)
        up_low = sb("up_low", [P, UPW], f32r)
        down_high = sb("down_high", [P, DNW], f32r)
        down_low = sb("down_low", [P, DNW], f32r)
        x_raw = [sb(f"x_raw{n}", [P, HT, WID]) for n in range(2)]
        x_sum = [sb(f"x_sum{n}", [P, HT, WID]) for n in range(2)]
        x_high = [sb(f"x_high{n}", [P, HT, WID], f32r) for n in range(2)]
        x_low = [sb(f"x_low{n}", [P, HT, WID], f32r) for n in range(2)]
        a_high = [sb(f"a_high{n}", [P, HT, UP], f32r) for n in range(2)]
        a_low = [sb(f"a_low{n}", [P, HT, UP], f32r) for n in range(2)]
        leak = [sb(f"leak{i}", [P, UP]) for i in range(2)]
        z = [sb(f"z{n}", [P, UT, UP]) for n in range(2)]
        p_high = [sb(f"p_high{n}", [P, UT, H], f32r) for n in range(2)]
        p_low = [sb(f"p_low{n}", [P, UT, H], f32r) for n in range(2)]
        o_out = [sb(f"o_out{n}", [P, HT, WID]) for n in range(2)]
        f_rows = sb("f_rows", [ROWS, H + WID], f32r)

        a_ps = pb("a_ps", [P, HT, UP])
        y_ps = [pb(f"y_ps{i}", [P, UP]) for i in range(2)]
        p_ps = [pb(f"p_ps{i}", [P, 2, H]) for i in range(2)]
        o_ps = pb("o_ps", [P, HT, WID])
        f_ps = pb("f_ps", [P, HT, WID])

        params_loaded = sem("params_loaded")
        masks_made = sem("masks_made")
        setup_step = sem("setup_step")
        angle_ready = sem("angle_ready")
        trig_ready = sem("trig_ready")
        rows_ready = sem("rows_ready")
        rows_saved = sem("rows_saved")
        bands_ready = sem("bands_ready")
        f_rows_loaded = sem("f_rows_loaded")
        f_made = sem("f_made")
        x_loaded = [sem(f"x_loaded{n}") for n in range(2)]
        x_summed = sem("x_summed")
        x_high_done = sem("x_high_done")
        x_split = sem("x_split")
        a_made = sem("a_made")
        a_high_done = sem("a_high_done")
        a_split = sem("a_split")
        y_made = sem("y_made")
        leak_done = sem("leak_done")
        z_done = sem("z_done")
        p_made = sem("p_made")
        p_high_done = sem("p_high_done")
        p_split = sem("p_split")
        o_made = sem("o_made")
        o_copied = sem("o_copied")
        o_stored = [sem(f"o_stored{n}") for n in range(2)]

        def reached(eng, s, count):
            if not isinstance(count, int) or count > 0:
                eng.wait_ge(s, count)

        block = ctx.enter_context(nc.Block())

        @block.sync
        def _(sp):
            sp.dma_start(up_taps[:, :], up_filter.partition_broadcast(P)).then_inc(params_loaded, 16)
            sp.dma_start(down_taps[:, :], down_filter.partition_broadcast(P)).then_inc(params_loaded, 16)
            sp.dma_start(w_cols[:, :, :], W.rearrange("(p t) k -> p t k", t=CT)).then_inc(params_loaded, 16)
            sp.dma_start(b_cols[:, :], b.rearrange("(p t) -> p t", t=CT)).then_inc(params_loaded, 16)
            sp.dma_start(bias_cols[:, :], bias.rearrange("(p t) -> p t", t=CT)).then_inc(params_loaded, 16)

            def load_x(c, n):
                sp.dma_start(x_raw[n][:, :, :],
                             x[n, c, :, :].rearrange("(t p) w -> p t w", p=P)).then_inc(x_loaded[n], 16)

            def load_f_rows(c):
                sp.dma_start(f_rows[:, :].bitcast(f32), trig_dram[c, :, :]).then_inc(f_rows_loaded, 16)

            def store(c, n):
                sp.dma_start(out[n, c, :, :].rearrange("(t p) w -> p t w", p=P),
                             o_out[n][:, :, :]).then_inc(o_stored[n], 16)

            load_x(0, 0)
            load_x(0, 1)
            with sp.Fori(0, CT) as t:
                sp.wait_ge(rows_ready, t + 1)
                sp.dma_start(trig_store[t, :, :], trig_rows[:, :, :].rearrange("p r n -> p (r n)").bitcast(f32)
                             ).then_inc(rows_saved, 16)
            sp.wait_ge(rows_saved, 16 * CT)
            load_f_rows(0)
            sp.wait_ge(f_made, 1)
            load_f_rows(1)
            for n in range(2):
                sp.wait_ge(x_summed, n + 1)
                load_x(1, n)

            def step(c, more_rows, more_x, stores=True):
                if more_rows:
                    sp.wait_ge(f_made, c + 2)
                    load_f_rows(c + 2)
                for n in range(2):
                    if more_x:
                        sp.wait_ge(x_summed, 2 * c + n + 3)
                        load_x(c + 2, n)
                    if stores:
                        sp.wait_ge(o_copied, 2 * c + n - 1)
                        store(c - 1, n)

            step(0, True, True, stores=False)
            with sp.Fori(1, C - 2) as c:
                step(c, True, True)
            step(C - 2, False, False)
            step(C - 1, False, False)
            step(C, False, False)
            for n in range(2):
                sp.wait_ge(o_stored[n], 16 * C)

        @block.gpsimd
        def _(pool):
            nc.gpsimd.memset(up_ones[:, :], 0.0).then_inc(masks_made, 1)
            nc.gpsimd.memset(down_ones[:, :], 0.0).then_inc(masks_made, 1)
            pool.wait_ge(masks_made, 2)
            nc.gpsimd.affine_select(out=up_ones[:, :], in_=up_ones[:, :], compare_op=ALU.not_equal, fill=1.0,
                                    base=-12, pattern=[[1, 280]], channel_multiplier=-2).then_inc(masks_made, 1)
            nc.gpsimd.affine_select(out=down_ones[:, :], in_=down_ones[:, :], compare_op=ALU.not_equal, fill=1.0,
                                    base=-13, pattern=[[1, 156]], channel_multiplier=-1).then_inc(masks_made, 1)
            nc.gpsimd.iota(coord[:, :], pattern=[[1, H]], base=0, channel_multiplier=0,
                           allow_small_or_imprecise_dtypes=True).then_inc(masks_made, 1)

            def split_x(m, n):
                pool.wait_ge(x_high_done, m + 1)
                nc.gpsimd.tensor_tensor(x_low[n][:, :, :], x_sum[n][:, :, :], x_high[n][:, :, :].bitcast(f32),
                                        ALU.subtract).then_inc(x_split, 1)

            with pool.Fori(0, C) as c:
                for n in range(2):
                    split_x(2 * c + n, n)

        @block.scalar
        def _(act):
            with act.Fori(0, CT) as t:
                act.wait_ge(angle_ready, t + 1)
                nc.scalar.activation(trig[:, :, :, :].rearrange("p a b n -> p (a b n)"),
                                     angle[:, :, :].rearrange("p a n -> p (a n)"), ACT.Sin).then_inc(trig_ready, 1)

            def high_a(m, n):
                act.wait_ge(a_made, m + 1)
                nc.scalar.copy(a_high[n][:, :, :], a_ps[:, :, :]).then_inc(a_high_done, 1)

            def leaky(m, i):
                act.wait_ge(y_made, 4 * m + i + 1)
                nc.scalar.mul(leak[i % 2][:, :], y_ps[i % 2][:, :], SLOPE * GAIN).then_inc(leak_done, 1)

            def high_p(m, n, i):
                act.wait_ge(p_made, 2 * m + i + 1)
                nc.scalar.copy(p_high[n][:, 2 * i:2 * i + 2, :], p_ps[i][:, :, :]).then_inc(p_high_done, 1)

            def copy_o(m, n, stored):
                act.wait_ge(o_made, m + 1)
                reached(act, o_stored[n], stored)
                nc.scalar.copy(o_out[n][:, :, :], o_ps[:, :, :]).then_inc(o_copied, 1)

            def slot(c, n, a_next=True, y=True, p=True, o=True):
                m = 2 * c + n
                if a_next:
                    high_a(m + 1, 1 - n)
                if y:
                    leaky(m, 0)
                    leaky(m, 1)
                if p:
                    high_p(m - 1, 1 - n, 0)
                if y:
                    leaky(m, 2)
                    leaky(m, 3)
                if p:
                    high_p(m - 1, 1 - n, 1)
                if o:
                    copy_o(m - 2, n, 16 * (c - 1))

            high_a(0, 0)
            slot(0, 0, p=False, o=False)
            slot(0, 1, o=False)
            with act.Fori(1, C - 1) as c:
                slot(c, 0)
                slot(c, 1)
            slot(C - 1, 0)
            slot(C - 1, 1, a_next=False)
            slot(C, 0, a_next=False, y=False)
            slot(C, 1, a_next=False, y=False, p=False)

        @block.vector
        def _(dve):
            done = [0]

            def chain(instruction, base=0):
                done[0] += 1
                instruction.then_inc(setup_step, 1)
                dve.wait_ge(setup_step, base + done[0])

            dve.wait_ge(params_loaded, 80)
            dve.wait_ge(masks_made, 5)
            for tap in range(TAPS):
                lo = TAPS - 1 - tap
                up_diag = up_ones[:, lo:lo + UPW]
                dn_diag = down_ones[:, lo:lo + 2 * DNW].rearrange("p (m s) -> p m s", s=2)[:, :, 0]
                if tap == 0:
                    nc.vector.tensor_scalar(up_band[:, :], up_diag, up_taps[:, 0:1], None, ALU.mult)
                    chain(nc.vector.tensor_scalar(down_band[:, :], dn_diag, down_taps[:, 0:1], None, ALU.mult))
                else:
                    nc.vector.scalar_tensor_tensor(up_band[:, :], up_diag, up_taps[:, tap:tap + 1], up_band[:, :],
                                                   ALU.mult, ALU.add)
                    chain(nc.vector.scalar_tensor_tensor(down_band[:, :], dn_diag, down_taps[:, tap:tap + 1],
                                                         down_band[:, :], ALU.mult, ALU.add))
            chain(nc.vector.tensor_scalar(up_band[:, :], up_band[:, :], 2.0, None, ALU.mult))
            nc.vector.tensor_copy(up_high[:, :], up_band[:, :])
            chain(nc.vector.tensor_copy(down_high[:, :], down_band[:, :]))
            nc.vector.tensor_tensor(up_low[:, :], up_band[:, :], up_high[:, :].bitcast(f32),
                                    ALU.subtract).then_inc(bands_ready, 1)
            nc.vector.tensor_tensor(down_low[:, :], down_band[:, :], down_high[:, :].bitcast(f32),
                                    ALU.subtract).then_inc(bands_ready, 1)
            nc.vector.memset(ones[:, :], 1.0)
            nc.vector.memset(trig_rows[:, 8:10, 0:H].bitcast(f32), 1.0)
            nc.vector.tensor_copy(bias_high[:, :], bias_cols[:, :])
            chain(nc.vector.tensor_scalar(coord[:, :], coord[:, :], 2.0 / (H - 1), -1.0, ALU.mult, ALU.add))
            chain(nc.vector.tensor_tensor(bias_low[:, :], bias_cols[:, :], bias_high[:, :].bitcast(f32),
                                          ALU.subtract))

            before = done[0]
            CHAINED = 9

            with dve.Fori(0, CT) as t:
                done[0] = 0
                base = t * CHAINED + before
                nc.vector.tensor_scalar(phase[:, 0, :], coord[:, :], w_cols[:, bass.ds(t, 1), 1], b_cols[:, bass.ds(t, 1)],
                                        ALU.mult, ALU.add)
                chain(nc.vector.tensor_scalar(phase[:, 1, :], coord[:, :], w_cols[:, bass.ds(t, 1), 0], None, ALU.mult),
                      base)
                flat = phase[:, :, :].rearrange("p a n -> p (a n)")
                nc.vector.tensor_scalar(turns[:, 0, :], flat, 1.0 / (2 * math.pi), None, ALU.mult)
                chain(nc.vector.tensor_scalar(turns[:, 1, :], flat, 1.0 / (2 * math.pi), 0.25, ALU.mult, ALU.add), base)
                chain(nc.vector.tensor_scalar(turns[:, :, :], turns[:, :, :], ROUND, -ROUND, ALU.add, ALU.add), base)
                for part in (TWO_PI_A, TWO_PI_B, TWO_PI_C):
                    for k in range(2):
                        last = nc.vector.scalar_tensor_tensor(
                            angle[:, k, :], turns[:, k, :], -part, flat if part == TWO_PI_A else angle[:, k, :],
                            ALU.mult, ALU.add)
                    chain(last, base)
                chain(nc.vector.tensor_scalar(angle[:, 1, :], angle[:, 1, :], math.pi / 2, None, ALU.add), base)
                nc.vector.tensor_scalar(angle[:, :, :], angle[:, :, :], -PI_DOWN, PI_DOWN, ALU.max,
                                        ALU.min).then_inc(angle_ready, 1)
                dve.wait_ge(trig_ready, t + 1)
                first = {0: 0, 1: 4}
                for k in range(2):
                    side_y = trig_rows[:, first[k]:first[k] + 4, 0:H].rearrange("p (a s) n -> p a s n", s=2)
                    other = first[1 - k]
                    side_x = trig_rows[:, other:other + 4, H:H + WID]
                    for a in range(2):
                        nc.vector.tensor_copy(side_y[:, a, 0, :], trig[:, k, 0, :])
                        nc.vector.tensor_copy(side_x[:, a, :], trig[:, k, 1, :])
                nc.vector.tensor_scalar(trig_rows[:, 8, H:H + WID], ones[:, :], bias_high[:, bass.ds(t, 1)].bitcast(f32),
                                        None, ALU.mult)
                chain(nc.vector.tensor_scalar(trig_rows[:, 9, H:H + WID], ones[:, :], bias_low[:, bass.ds(t, 1)],
                                              None, ALU.mult), base)
                for k in range(2):
                    side_y = trig_rows[:, first[k]:first[k] + 4, 0:H].rearrange("p (a s) n -> p a s n", s=2)
                    other = first[1 - k]
                    side_x = trig_rows[:, other:other + 4, H:H + WID]
                    for a in range(2):
                        nc.vector.tensor_tensor(side_y[:, a, 1, :], trig[:, k, 0, :],
                                                side_y[:, a, 0, :].bitcast(f32), ALU.subtract)
                        last = nc.vector.tensor_tensor(side_x[:, 2 + a, :], trig[:, k, 1, :],
                                                       side_x[:, a, :].bitcast(f32), ALU.subtract)
                chain(last, base)
                last_done = done[0]
                assert last_done == CHAINED, last_done
                nc.vector.tensor_copy(turns[:, 0, 0:1], ones[:, 0:1]).then_inc(rows_ready, 1)
                dve.wait_ge(rows_saved, 16 * t + 16)

            def sum_x(c, n):
                m = 2 * c + n
                dve.wait_ge(x_loaded[n], 16 * c + 16)
                if n == 0:
                    dve.wait_ge(f_made, c + 1)
                nc.vector.tensor_tensor(x_sum[n][:, :, :], x_raw[n][:, :, :], f_ps[:, :, :],
                                        ALU.add).then_inc(x_summed, 1)

            def high_x(m, n):
                dve.wait_ge(x_summed, m + 1)
                nc.vector.tensor_copy(x_high[n][:, :, :], x_sum[n][:, :, :]).then_inc(x_high_done, 1)

            def low_a(m, n):
                dve.wait_ge(a_high_done, m + 1)
                nc.vector.tensor_tensor(a_low[n][:, :, :], a_ps[:, :, :], a_high[n][:, :, :].bitcast(f32),
                                        ALU.subtract).then_inc(a_split, 1)

            def leaky(m, n, i):
                dve.wait_ge(leak_done, 4 * m + i + 1)
                nc.vector.scalar_tensor_tensor(z[n][:, i, :], y_ps[i % 2][:, :], GAIN, leak[i % 2][:, :],
                                               ALU.mult, ALU.max).then_inc(z_done, 1)

            def low_p(m, n, i):
                dve.wait_ge(p_high_done, 2 * m + i + 1)
                nc.vector.tensor_tensor(p_low[n][:, 2 * i:2 * i + 2, :], p_ps[i][:, :, :],
                                        p_high[n][:, 2 * i:2 * i + 2, :].bitcast(f32),
                                        ALU.subtract).then_inc(p_split, 1)

            def slot(c, n, a_next=True, y=True, p=True, x_next=True):
                m = 2 * c + n
                if a_next:
                    low_a(m + 1, 1 - n)
                if y:
                    leaky(m, n, 0)
                    leaky(m, n, 1)
                if p:
                    low_p(m - 1, 1 - n, 0)
                if x_next:
                    sum_x(c + 1, n)
                if y:
                    leaky(m, n, 2)
                if x_next:
                    high_x(m + 2, n)
                if y:
                    leaky(m, n, 3)
                if p:
                    low_p(m - 1, 1 - n, 1)

            for n in range(2):
                sum_x(0, n)
                high_x(n, n)
            low_a(0, 0)
            slot(0, 0, p=False)
            slot(0, 1)
            with dve.Fori(1, C - 1) as c:
                slot(c, 0)
                slot(c, 1)
            slot(C - 1, 0, x_next=False)
            slot(C - 1, 1, a_next=False, x_next=False)
            slot(C, 0, a_next=False, y=False, x_next=False)

        @block.tensor
        def _(pe):
            def product(parts, spans, out_ps, lhs, first):
                for t, (lo, hi, at) in enumerate(spans):
                    for k, (data, band) in enumerate(parts):
                        last = nc.tensor.matmul(out_ps[:, lo:hi], lhs(data, t), band[:, at:at + hi - lo],
                                                start=first and t == 0 and k == 0,
                                                stop=t == len(spans) - 1 and k == len(parts) - 1,
                                                skip_group_check=True)
                return last

            def sines(c):
                pe.wait_ge(f_rows_loaded, 16 * c + 16)
                reached(pe, x_summed, 2 * c)
                for t in range(HT):
                    last = nc.tensor.matmul(f_ps[:, t, :], f_rows[:, t * P:(t + 1) * P], f_rows[:, H:H + WID],
                                            start=True, stop=True)
                last.then_inc(f_made, 1)

            def up_rows(m, n):
                pe.wait_ge(x_split, m + 1)
                reached(pe, a_split, m)
                for t in range(HT):
                    last = product([(x_low[n], up_high), (x_high[n], up_low), (x_high[n], up_high)], UP_SPAN,
                                   a_ps[:, t, :], lambda d, k, t=t: d[:, k, t * P:(t + 1) * P], True)
                last.then_inc(a_made, 1)

            def up_cols(m, n, i):
                if i == 0:
                    pe.wait_ge(a_split, m + 1)
                reached(pe, z_done, 4 * m + i - 1)
                product([(a_low[n], up_high), (a_high[n], up_low), (a_high[n], up_high)], UP_SPAN,
                        y_ps[i % 2][:, :], lambda d, k: d[:, k, i * P:(i + 1) * P], True).then_inc(y_made, 1)

            def down_rows(m, n, j):
                if j == 0:
                    pe.wait_ge(z_done, 4 * m + 4)
                if j % 2 == 0:
                    reached(pe, p_split, 2 * m + j // 2 - 1)
                last = product([(z[n], down_band)], DN_SPAN, p_ps[j // 2][:, j % 2, :],
                               lambda d, k: d[:, k, j * P:(j + 1) * P], j % 2 == 0)
                if j % 2 == 1:
                    last.then_inc(p_made, 1)

            def down_cols(m, n):
                pe.wait_ge(p_split, 2 * m + 2)
                reached(pe, o_copied, m)
                for t in range(HT):
                    last = product([(p_low[n], down_high), (p_high[n], down_low), (p_high[n], down_high)], DN_SPAN,
                                   o_ps[:, t, :], lambda d, k, t=t: d[:, k, t * P:(t + 1) * P], t == 0)
                last.then_inc(o_made, 1)

            def slot(c, n, a_next=True, f_next=True, y=True, p=True, o=True):
                m = 2 * c + n
                if a_next:
                    up_rows(m + 1, 1 - n)
                if f_next and n == 0:
                    sines(c + 1)
                for i in range(UT):
                    if y:
                        up_cols(m, n, i)
                    if p:
                        down_rows(m - 1, 1 - n, i)
                if o:
                    down_cols(m - 2, n)

            pe.wait_ge(bands_ready, 2)
            sines(0)
            up_rows(0, 0)
            slot(0, 0, p=False, o=False)
            slot(0, 1, o=False)
            with pe.Fori(1, C - 1) as c:
                slot(c, 0)
                slot(c, 1)
            slot(C - 1, 0, f_next=False)
            slot(C - 1, 1, a_next=False)
            slot(C, 0, a_next=False, f_next=False, y=False)
            slot(C, 1, a_next=False, y=False, p=False)


_INS = ["x", "L0_conv_W", "L0_conv_b", "L1_conv_bias", "L1_conv_up_filter", "L1_conv_down_filter"]


def kernel(**inputs):
    import numpy as _np
    import concourse.bacc as _bacc
    from concourse import mybir as _mybir
    from concourse.bass_utils import run_bass_kernel_spmd as _run

    nc = _bacc.Bacc("TRN2", target_bir_lowering=False, num_devices=1)
    arrays, args = {}, []
    for name in _INS:
        a = _np.ascontiguousarray(inputs[name])
        arrays[f"in_{name}_dram"] = a
        args.append(nc.dram_tensor(f"in_{name}_dram", a.shape, _mybir.dt.from_np(a.dtype), kind="ExternalInput").ap())
    shape = inputs["x"].shape
    args.append(nc.dram_tensor("out_dram", shape, _mybir.dt.float32, kind="ExternalOutput").ap())
    filtered_lrelu_kernel(nc, *args)
    r = _run(nc, [arrays], core_ids=[0])
    return r.results[0]["out_dram"]
```

```python
import concourse.bass as bass
from concourse import mybir
from contextlib import ExitStack
import math


def filtered_lrelu_kernel(nc, x, W, b, bias, up_filter, down_filter, out):
    f32 = mybir.dt.float32
    f32r = mybir.dt.float32r
    ALU = mybir.AluOpType
    ACT = mybir.ActivationFunctionType

    BATCH, C, H, WID = x.shape
    TAPS = up_filter.shape[0]
    P = 128
    assert BATCH == 2 and H == 2 * P and WID == 2 * P and TAPS == 12
    HT = H // P
    UP = 2 * H
    UT = UP // P

    UPW = 268
    UP_SPAN = [(0, 262, 6), (250, 512, 0)]
    DNW = 72
    DN_SPAN = [(0, 68, 4), (60, 132, 0), (124, 196, 0), (188, 256, 0)]

    PE_CHANNELS = 3
    assert (C - 2) % PE_CHANNELS == 0

    SLOPE = 0.2
    GAIN = math.sqrt(2.0)

    TWO_PI_A = 6.28125
    TWO_PI_B = 2.0 * math.pi - TWO_PI_A
    ROUND = 1.5 * 2.0 ** 23
    PI_DOWN = 3.1415925

    CP = min(P, C)
    CT = C // CP
    ROWS = 10

    trig_dram = nc.dram_tensor("trig_dram", [C, ROWS, H + WID], f32).ap()
    trig_store = trig_dram.rearrange("(t p) r n -> t p r n", t=CT)

    ctx = ExitStack()
    with ctx:
        def sb(name, shape, dt=f32):
            return ctx.enter_context(nc.sbuf_tensor(name, shape, dt))

        def pb(name, shape):
            return ctx.enter_context(nc.psum_tensor(name, shape, f32))

        def sem(name):
            return ctx.enter_context(nc.semaphore(name))

        up_taps = sb("up_taps", [P, TAPS])
        down_taps = sb("down_taps", [P, TAPS])
        w_cols = sb("w_cols", [CP, CT, 2])
        b_cols = sb("b_cols", [CP, CT])
        b_quarter = sb("b_quarter", [CP, CT])
        bias_cols = sb("bias_cols", [CP, CT])
        bias_high = sb("bias_high", [CP, CT], f32r)
        bias_low = sb("bias_low", [CP, CT])
        up_ones = sb("up_ones", [P, 280])
        down_ones = sb("down_ones", [P, 156])
        up_band = sb("up_band", [P, UPW])
        down_band = sb("down_band", [P, DNW])
        coord = sb("coord", [CP, H])
        ones = sb("ones", [CP, 2, H])
        phase = sb("phase", [CP, 4, H])
        turns = sb("turns", [CP, 4, H])
        angle = sb("angle", [CP, 4, H])
        trig = sb("trig", [CP, 4, H])
        trig_parts = sb("trig_parts", [CP, CT, 2, 4, H], f32r)
        bias_wide = sb("bias_wide", [CP, CT, 2, WID], f32r)
        up_high = sb("up_high", [P, UPW], f32r)
        up_low = sb("up_low", [P, UPW], f32r)
        x_raw = [sb(f"x_raw{n}", [P, HT, WID]) for n in range(2)]
        x_sum = [sb(f"x_sum{n}", [P, HT, WID]) for n in range(2)]
        x_high = [sb(f"x_high{n}", [P, HT, WID], f32r) for n in range(2)]
        x_low = [sb(f"x_low{n}", [P, HT, WID], f32r) for n in range(2)]
        a_high = [sb(f"a_high{n}", [P, HT, UP], f32r) for n in range(2)]
        a_low = [sb(f"a_low{n}", [P, HT, UP], f32r) for n in range(2)]
        leak = [sb(f"leak{i}", [P, UP]) for i in range(2)]
        z = [sb(f"z{n}", [P, UT, UP]) for n in range(2)]
        p_rows = [sb(f"p_rows{n}", [P, UT, H]) for n in range(2)]
        o_out = [sb(f"o_out{n}", [P, HT, WID]) for n in range(2)]
        f_rows = sb("f_rows", [ROWS, H + WID], f32r)

        a_ps = pb("a_ps", [P, HT, UP])
        y_ps = [pb(f"y_ps{i}", [P, UP]) for i in range(2)]
        p_ps = [pb(f"p_ps{i}", [P, 2, H]) for i in range(2)]
        o_ps = pb("o_ps", [P, HT, WID])
        f_ps = pb("f_ps", [P, HT, WID])

        params_loaded = sem("params_loaded")
        masks_made = sem("masks_made")
        setup_step = sem("setup_step")
        angle_ready = sem("angle_ready")
        trig_ready = sem("trig_ready")
        rows_ready = sem("rows_ready")
        bias_made = sem("bias_made")
        bias_rows_ready = sem("bias_rows_ready")
        first_rows_saved = sem("first_rows_saved")
        other_rows_saved = sem("other_rows_saved")
        bands_ready = sem("bands_ready")
        f_rows_loaded = sem("f_rows_loaded")
        f_made = sem("f_made")
        x_loaded = [sem(f"x_loaded{n}") for n in range(2)]
        x_summed = sem("x_summed")
        x_high_done = sem("x_high_done")
        x_split = sem("x_split")
        a_made = sem("a_made")
        a_high_done = sem("a_high_done")
        a_split = sem("a_split")
        y_made = sem("y_made")
        leak_done = sem("leak_done")
        z_done = sem("z_done")
        p_made = sem("p_made")
        p_copied = sem("p_copied")
        o_made = sem("o_made")
        o_copied = sem("o_copied")
        o_stored = [sem(f"o_stored{n}") for n in range(2)]

        def reached(eng, s, count):
            if not isinstance(count, int) or count > 0:
                eng.wait_ge(s, count)

        block = ctx.enter_context(nc.Block())

        @block.sync
        def _(sp):
            sp.dma_start(up_taps[:, :], up_filter.partition_broadcast(P)).then_inc(params_loaded, 16)
            sp.dma_start(down_taps[:, :], down_filter.partition_broadcast(P)).then_inc(params_loaded, 16)
            with nc.allow_non_contiguous_dma(reason="a few values per channel"):
                sp.dma_start(w_cols[:, :, :], W.rearrange("(t p) k -> p t k", t=CT)).then_inc(params_loaded, 16)
                sp.dma_start(b_cols[:, :], b.rearrange("(t p) -> p t", t=CT)).then_inc(params_loaded, 16)
                sp.dma_start(bias_cols[:, :], bias.rearrange("(t p) -> p t", t=CT)).then_inc(params_loaded, 16)

            def load_x(c, n):
                sp.dma_start(x_raw[n][:, :, :],
                             x[n, c, :, :].rearrange("(t p) w -> p t w", p=P)).then_inc(x_loaded[n], 16)

            def load_f_rows(c):
                sp.dma_start(f_rows[:, :].bitcast(f32), trig_dram[c, :, :]).then_inc(f_rows_loaded, 16)

            def store(c, n):
                sp.dma_start(out[n, c, :, :].rearrange("(t p) w -> p t w", p=P),
                             o_out[n][:, :, :]).then_inc(o_stored[n], 16)

            load_x(0, 0)
            load_x(0, 1)

            def save_rows(t, saved):
                sp.wait_ge(bias_rows_ready, t + 1)
                rows = trig_store[t, :, :, :]
                sp.dma_start(rows[:, 8:10, 0:H], ones[:, :, :]).then_inc(saved, 16)
                sp.dma_start(rows[:, 8:10, H:H + WID],
                             bias_wide[:, bass.ds(t, 1), :, :].rearrange("p t a n -> p (t a) n").bitcast(f32)
                             ).then_inc(saved, 16)
                sp.wait_ge(rows_ready, t + 1)
                parts = trig_parts[:, bass.ds(t, 1), :, :, :].rearrange("p t s (k d) n -> p (t s) k d n",
                                                                        d=2).bitcast(f32)
                for a in range(2):
                    for s in range(2):
                        at = 4 * a + 2 * s
                        sp.dma_start(rows[:, at:at + 2, 0:H], parts[:, s, :, 0, :]).then_inc(saved, 16)
                        sp.dma_start(rows[:, at:at + 2, H:H + WID], parts[:, a, :, 1, :]).then_inc(saved, 16)

            SAVES = 10
            save_rows(0, first_rows_saved)
            sp.wait_ge(first_rows_saved, 16 * SAVES)
            load_f_rows(0)
            if CT > 1:
                with sp.Fori(1, CT) as t:
                    save_rows(t, other_rows_saved)
                sp.wait_ge(other_rows_saved, 16 * SAVES * (CT - 1))
            sp.wait_ge(f_made, 1)
            load_f_rows(1)
            for n in range(2):
                sp.wait_ge(x_summed, n + 1)
                load_x(1, n)

            def step(c, more_rows, more_x, stores=True):
                if more_rows:
                    sp.wait_ge(f_made, c + 2)
                    load_f_rows(c + 2)
                for n in range(2):
                    if more_x:
                        sp.wait_ge(x_summed, 2 * c + n + 3)
                        load_x(c + 2, n)
                    if stores:
                        sp.wait_ge(o_copied, 2 * c + n - 1)
                        store(c - 1, n)

            step(0, True, True, stores=False)
            with sp.Fori(1, C - 2) as c:
                step(c, True, True)
            step(C - 2, False, False)
            step(C - 1, False, False)
            step(C, False, False)
            for n in range(2):
                sp.wait_ge(o_stored[n], 16 * C)

        @block.gpsimd
        def _(pool):
            nc.gpsimd.memset(up_ones[:, :], 0.0).then_inc(masks_made, 1)
            nc.gpsimd.memset(down_ones[:, :], 0.0).then_inc(masks_made, 1)
            pool.wait_ge(masks_made, 2)
            nc.gpsimd.affine_select(out=up_ones[:, :], in_=up_ones[:, :], compare_op=ALU.not_equal, fill=1.0,
                                    base=-12, pattern=[[1, 280]], channel_multiplier=-2).then_inc(masks_made, 1)
            nc.gpsimd.affine_select(out=down_ones[:, :], in_=down_ones[:, :], compare_op=ALU.not_equal, fill=1.0,
                                    base=-13, pattern=[[1, 156]], channel_multiplier=-1).then_inc(masks_made, 1)
            nc.gpsimd.iota(coord[:, :], pattern=[[1, H]], base=0, channel_multiplier=0,
                           allow_small_or_imprecise_dtypes=True).then_inc(masks_made, 1)

            pool.wait_ge(bias_made, 1)
            for t in range(CT):
                nc.gpsimd.tensor_scalar(bias_wide[:, t, 0, :], ones[:, 0, :], bias_high[:, t:t + 1].bitcast(f32),
                                        None, ALU.mult)
                nc.gpsimd.tensor_scalar(bias_wide[:, t, 1, :], ones[:, 0, :], bias_low[:, t:t + 1],
                                        None, ALU.mult).then_inc(bias_rows_ready, 1)

            def split_x(m, n):
                pool.wait_ge(x_high_done, m + 1)
                nc.gpsimd.tensor_tensor(x_low[n][:, :, :], x_sum[n][:, :, :], x_high[n][:, :, :].bitcast(f32),
                                        ALU.subtract).then_inc(x_split, 1)

            with pool.Fori(0, C) as c:
                for n in range(2):
                    split_x(2 * c + n, n)

        @block.scalar
        def _(act):
            with act.Fori(0, CT) as t:
                act.wait_ge(angle_ready, t + 1)
                nc.scalar.activation(trig[:, :, :], angle[:, :, :], ACT.Sin).then_inc(trig_ready, 1)

            def high_a(m, n):
                act.wait_ge(a_made, m + 1)
                nc.scalar.copy(a_high[n][:, :, :], a_ps[:, :, :]).then_inc(a_high_done, 1)

            def leaky(m, i):
                act.wait_ge(y_made, 4 * m + i + 1)
                nc.scalar.mul(leak[i % 2][:, :], y_ps[i % 2][:, :], SLOPE * GAIN).then_inc(leak_done, 1)

            def copy_o(m, n, stored):
                act.wait_ge(o_made, m + 1)
                reached(act, o_stored[n], stored)
                nc.scalar.copy(o_out[n][:, :, :], o_ps[:, :, :]).then_inc(o_copied, 1)

            def slot(c, n, a_next=True, y=True, o=True):
                m = 2 * c + n
                if y:
                    leaky(m, 0)
                if a_next:
                    high_a(m + 1, 1 - n)
                if y:
                    leaky(m, 1)
                    leaky(m, 2)
                    leaky(m, 3)
                if o:
                    copy_o(m - 2, n, 16 * (c - 1))

            high_a(0, 0)
            slot(0, 0, o=False)
            slot(0, 1, o=False)
            slot(1, 0)
            slot(1, 1)
            with act.Fori(2, C - 1) as c:
                slot(c, 0)
                slot(c, 1)
            slot(C - 1, 0)
            slot(C - 1, 1, a_next=False)
            slot(C, 0, a_next=False, y=False)
            slot(C, 1, a_next=False, y=False)

        @block.vector
        def _(dve):
            done = [0]

            def chain(instruction, base=0):
                done[0] += 1
                instruction.then_inc(setup_step, 1)
                dve.wait_ge(setup_step, base + done[0])

            dve.wait_ge(params_loaded, 80)
            dve.wait_ge(masks_made, 5)
            nc.vector.memset(ones[:, :, :], 1.0)
            nc.vector.tensor_copy(bias_high[:, :], bias_cols[:, :])
            nc.vector.tensor_scalar(b_quarter[:, :], b_cols[:, :], math.pi / 2, None, ALU.add)
            chain(nc.vector.tensor_scalar(coord[:, :], coord[:, :], 2.0 / (H - 1), -1.0, ALU.mult, ALU.add))
            nc.vector.tensor_tensor(bias_low[:, :], bias_cols[:, :], bias_high[:, :].bitcast(f32),
                                    ALU.subtract).then_inc(bias_made, 1)

            CHAINED = 6

            def tables(t, before):
                done[0] = 0
                for q, offset in enumerate((b_cols[:, bass.ds(t, 1)], math.pi / 2, b_quarter[:, bass.ds(t, 1)], 0.0)):
                    last = nc.vector.tensor_scalar(phase[:, q, :], coord[:, :], w_cols[:, bass.ds(t, 1), 1 - q % 2],
                                                   offset, ALU.mult, ALU.add)
                chain(last, before)
                chain(nc.vector.tensor_scalar(turns[:, :, :], phase[:, :, :], 1.0 / (2 * math.pi), ROUND,
                                              ALU.mult, ALU.add), before)
                chain(nc.vector.tensor_scalar(turns[:, :, :], turns[:, :, :], -ROUND, None, ALU.add), before)
                chain(nc.vector.scalar_tensor_tensor(angle[:, :, :], turns[:, :, :], -TWO_PI_A, phase[:, :, :],
                                                     ALU.mult, ALU.add), before)
                chain(nc.vector.scalar_tensor_tensor(angle[:, :, :], turns[:, :, :], -TWO_PI_B, angle[:, :, :],
                                                     ALU.mult, ALU.add), before)
                nc.vector.tensor_scalar(angle[:, :, :], angle[:, :, :], -PI_DOWN, PI_DOWN, ALU.max,
                                        ALU.min).then_inc(angle_ready, 1)
                dve.wait_ge(trig_ready, t + 1)
                parts = trig_parts[:, bass.ds(t, 1), :, :, :].rearrange("p t s q n -> p (t s) q n")
                chain(nc.vector.tensor_copy(parts[:, 0, :, :], trig[:, :, :]), before)
                nc.vector.tensor_tensor(parts[:, 1, :, :], trig[:, :, :], parts[:, 0, :, :].bitcast(f32),
                                        ALU.subtract).then_inc(rows_ready, 1)
                assert done[0] == CHAINED, done[0]

            before = done[0]
            tables(0, before)
            done[0] = before + CHAINED
            for tap in range(TAPS):
                lo = TAPS - 1 - tap
                up_diag = up_ones[:, lo:lo + UPW]
                dn_diag = down_ones[:, lo:lo + 2 * DNW].rearrange("p (m s) -> p m s", s=2)[:, :, 0]
                if tap == 0:
                    nc.vector.tensor_scalar(up_band[:, :], up_diag, up_taps[:, 0:1], None, ALU.mult)
                    chain(nc.vector.tensor_scalar(down_band[:, :], dn_diag, down_taps[:, 0:1], None, ALU.mult))
                else:
                    nc.vector.scalar_tensor_tensor(up_band[:, :], up_diag, up_taps[:, tap:tap + 1], up_band[:, :],
                                                   ALU.mult, ALU.add)
                    chain(nc.vector.scalar_tensor_tensor(down_band[:, :], dn_diag, down_taps[:, tap:tap + 1],
                                                         down_band[:, :], ALU.mult, ALU.add))
            chain(nc.vector.tensor_scalar(up_band[:, :], up_band[:, :], 2.0, None, ALU.mult))
            chain(nc.vector.tensor_copy(up_high[:, :], up_band[:, :]))
            nc.vector.tensor_tensor(up_low[:, :], up_band[:, :], up_high[:, :].bitcast(f32),
                                    ALU.subtract).then_inc(bands_ready, 1)
            if CT > 1:
                before = done[0]
                with dve.Fori(1, CT) as t:
                    tables(t, t * CHAINED + (before - CHAINED))

            def sum_x(c, n):
                m = 2 * c + n
                dve.wait_ge(x_loaded[n], 16 * c + 16)
                if n == 0:
                    dve.wait_ge(f_made, c + 1)
                nc.vector.tensor_tensor(x_sum[n][:, :, :], x_raw[n][:, :, :], f_ps[:, :, :],
                                        ALU.add).then_inc(x_summed, 1)

            def high_x(m, n):
                dve.wait_ge(x_summed, m + 1)
                nc.vector.tensor_copy(x_high[n][:, :, :], x_sum[n][:, :, :]).then_inc(x_high_done, 1)

            def low_a(m, n):
                dve.wait_ge(a_high_done, m + 1)
                nc.vector.tensor_tensor(a_low[n][:, :, :], a_ps[:, :, :], a_high[n][:, :, :].bitcast(f32),
                                        ALU.subtract).then_inc(a_split, 1)

            def leaky(m, n, i):
                dve.wait_ge(leak_done, 4 * m + i + 1)
                nc.vector.scalar_tensor_tensor(z[n][:, i, :], y_ps[i % 2][:, :], GAIN, leak[i % 2][:, :],
                                               ALU.mult, ALU.max).then_inc(z_done, 1)

            def copy_p(m, n, i):
                dve.wait_ge(p_made, 2 * m + i + 1)
                nc.vector.tensor_copy(p_rows[n][:, 2 * i:2 * i + 2, :], p_ps[i][:, :, :]).then_inc(p_copied, 1)

            def slot(c, n, a_next=True, y=True, p=True, x_next=True):
                m = 2 * c + n
                if y:
                    leaky(m, n, 0)
                if a_next:
                    low_a(m + 1, 1 - n)
                if y:
                    leaky(m, n, 1)
                if p:
                    copy_p(m - 1, 1 - n, 0)
                if x_next:
                    sum_x(c + 1, n)
                if y:
                    leaky(m, n, 2)
                if x_next:
                    high_x(m + 2, n)
                if y:
                    leaky(m, n, 3)
                if p:
                    copy_p(m - 1, 1 - n, 1)

            for n in range(2):
                sum_x(0, n)
                high_x(n, n)
            low_a(0, 0)
            slot(0, 0, p=False)
            slot(0, 1)
            with dve.Fori(1, C - 1) as c:
                slot(c, 0)
                slot(c, 1)
            slot(C - 1, 0, x_next=False)
            slot(C - 1, 1, a_next=False, x_next=False)
            slot(C, 0, a_next=False, y=False, x_next=False)

        @block.tensor
        def _(pe):
            def product(parts, spans, out_ps, lhs, first):
                for t, (lo, hi, at) in enumerate(spans):
                    for k, (data, band) in enumerate(parts):
                        last = nc.tensor.matmul(out_ps[:, lo:hi], lhs(data, t), band[:, at:at + hi - lo],
                                                start=first and t == 0 and k == 0,
                                                stop=t == len(spans) - 1 and k == len(parts) - 1,
                                                skip_group_check=True)
                return last

            def sines(c):
                pe.wait_ge(f_rows_loaded, 16 * c + 16)
                reached(pe, x_summed, 2 * c)
                for t in range(HT):
                    last = nc.tensor.matmul(f_ps[:, t, :], f_rows[:, t * P:(t + 1) * P], f_rows[:, H:H + WID],
                                            start=True, stop=True)
                last.then_inc(f_made, 1)

            def up_rows(m, n):
                pe.wait_ge(x_split, m + 1)
                reached(pe, a_split, m)
                for t in range(HT):
                    last = product([(x_low[n], up_high), (x_high[n], up_low), (x_high[n], up_high)], UP_SPAN,
                                   a_ps[:, t, :], lambda d, k, t=t: d[:, k, t * P:(t + 1) * P], True)
                last.then_inc(a_made, 1)

            def up_cols(m, n, i):
                if i == 0:
                    pe.wait_ge(a_split, m + 1)
                reached(pe, z_done, 4 * m + i - 1)
                product([(a_low[n], up_high), (a_high[n], up_low), (a_high[n], up_high)], UP_SPAN,
                        y_ps[i % 2][:, :], lambda d, k: d[:, k, i * P:(i + 1) * P], True).then_inc(y_made, 1)

            def down_rows(m, n, j):
                if j == 0:
                    pe.wait_ge(z_done, 4 * m + 4)
                if j % 2 == 0:
                    reached(pe, p_copied, 2 * m + j // 2 - 1)
                last = product([(z[n], down_band)], DN_SPAN, p_ps[j // 2][:, j % 2, :],
                               lambda d, k: d[:, k, j * P:(j + 1) * P], j % 2 == 0)
                if j % 2 == 1:
                    last.then_inc(p_made, 1)

            def down_cols(m, n):
                pe.wait_ge(p_copied, 2 * m + 2)
                reached(pe, o_copied, m)
                for t in range(HT):
                    last = product([(p_rows[n], down_band)], DN_SPAN,
                                   o_ps[:, t, :], lambda d, k, t=t: d[:, k, t * P:(t + 1) * P], t == 0)
                last.then_inc(o_made, 1)

            def slot(c, n, a_next=True, f_next=True, y=True, p=True, o=True):
                m = 2 * c + n
                if a_next:
                    up_rows(m + 1, 1 - n)
                if f_next and n == 0:
                    sines(c + 1)
                for i in range(UT):
                    if y:
                        up_cols(m, n, i)
                    if p:
                        down_rows(m - 1, 1 - n, i)
                if o:
                    down_cols(m - 2, n)

            pe.wait_ge(bands_ready, 1)
            sines(0)
            up_rows(0, 0)
            slot(0, 0, p=False, o=False)
            slot(0, 1, o=False)
            with pe.Fori(1, C - 1, PE_CHANNELS) as c:
                for k in range(PE_CHANNELS):
                    slot(c + k, 0)
                    slot(c + k, 1)
            slot(C - 1, 0, f_next=False)
            slot(C - 1, 1, a_next=False)
            slot(C, 0, a_next=False, f_next=False, y=False)
            slot(C, 1, a_next=False, y=False, p=False)


_INS = ["x", "L0_conv_W", "L0_conv_b", "L1_conv_bias", "L1_conv_up_filter", "L1_conv_down_filter"]


def kernel(**inputs):
    import numpy as _np
    import concourse.bacc as _bacc
    from concourse import mybir as _mybir
    from concourse.bass_utils import run_bass_kernel_spmd as _run

    nc = _bacc.Bacc("TRN2", target_bir_lowering=False, num_devices=1)
    arrays, args = {}, []
    for name in _INS:
        a = _np.ascontiguousarray(inputs[name])
        arrays[f"in_{name}_dram"] = a
        args.append(nc.dram_tensor(f"in_{name}_dram", a.shape, _mybir.dt.from_np(a.dtype), kind="ExternalInput").ap())
    shape = inputs["x"].shape
    args.append(nc.dram_tensor("out_dram", shape, _mybir.dt.float32, kind="ExternalOutput").ap())
    filtered_lrelu_kernel(nc, *args)
    r = _run(nc, [arrays], core_ids=[0])
    return r.results[0]["out_dram"]
```
